# Optimizing a Trainium2 kernel written in Bass

```python
import numpy as np
import jax
import jax.numpy as jnp

def _softmax(x, axis=-1):
    return jax.nn.softmax(x, axis=axis)

def _gelu(x):
    return jax.nn.gelu(x, approximate=True)

def _silu(x):
    return jax.nn.silu(x)

def _sigmoid(x):
    return jax.nn.sigmoid(x)

def _layernorm(x, axis=-1, eps=1e-05):
    m = jnp.mean(x, axis=axis, keepdims=True)
    v = jnp.var(x, axis=axis, keepdims=True)
    return (x - m) / jnp.sqrt(v + eps)

def _scatter_add(tgt, idx, src, axis=0):
    return tgt.at[idx].add(src)

def _segment_sum(src, seg, n):
    return jax.ops.segment_sum(src, seg, n)
kernel_name = 'mk_rec_standalone_d1_rec_r8_9c8af6'

def setup_inputs(seed: int=0):
    np.random.seed(seed)
    _w = jnp.asarray

    def _rec_inputs():
        import jax
        import jax.numpy as jnp
        _rk = jax.random.key(seed)
        r_x = -0.000153849 + 1.00027 * jax.random.normal(jax.random.fold_in(_rk, 1), (2048, 24, 128), jnp.float32)
        return r_x
    r_x = _rec_inputs()

    def _L0_rec_setup():
        import jax, jax.numpy as jnp
        import numpy as np
        import itertools
        key = jax.random.key(seed)
        k1, k2 = jax.random.split(key)
        B, F, E = (256, 24, 128)
        P = F * (F - 1) // 2
        x = jax.random.normal(k1, (B, F, E), dtype=jnp.float32)
        W = jax.random.normal(k2, (P, E, E), dtype=jnp.float32) * (1.0 / np.sqrt(E))
        return {'x': x, 'W': W}
    _L0_rec_all = _L0_rec_setup()
    _L0_rec_in = {k: v for k, v in _L0_rec_all.items() if k in ('W',)}
    del _L0_rec_all
    return {'r_x': r_x, 'L0_rec_W': _L0_rec_in['W']}

def reference(r_x, L0_rec_W):
    import jax
    import jax.numpy as jnp

    def _L0_rec_ref(x, W):
        import jax, jax.numpy as jnp
        import numpy as np
        import itertools
        F = x.shape[1]
        pairs = np.array(list(itertools.combinations(range(F), 2)), dtype=np.int32)
        pi, pj = (pairs[:, 0], pairs[:, 1])
        xi = x[:, pi, :]
        xj = x[:, pj, :]
        p = jnp.einsum('bpe,pef->bpf', xi, W) * xj
        return p
    y = _L0_rec_ref(r_x, L0_rec_W)
    return y

_drawn_inputs = setup_inputs


def setup_inputs(seed=0):
    import zlib

    import numpy as np

    out = dict(_drawn_inputs(seed))
    spreads = {}
    factors = {}
    for name, (base, spread) in spreads.items():
        noise = np.random.default_rng([zlib.crc32(name.encode()), seed]).standard_normal(out[name].shape)
        drawn = base * np.exp(spread * noise) if base else spread * noise
        out[name] = jnp.asarray(drawn.astype(out[name].dtype))
    for name, factor in factors.items():
        out[name] = (out[name] * factor).astype(out[name].dtype)
    return out
```

```python
import concourse.bass as bass
from concourse import mybir
from contextlib import ExitStack

P = 128
BANK_PAIRS = 4
PIECE_BANKS = 3
PIECE = BANK_PAIRS * PIECE_BANKS
UNIT_ROWS = 2
OUT_SLOTS = 6


class Phase:

    def __init__(self, first, last, fields, first_tile, tiles, units_before, chunks_before):
        self.rows = list(range(first, last))
        self.first_pair = sum(fields - 1 - i for i in range(first))
        pairs = [(i, j) for i in self.rows for j in range(i + 1, fields)]
        self.pairs = len(pairs)
        self.pieces = -(-self.pairs // PIECE)
        self.units = -(-len(self.rows) // UNIT_ROWS)
        self.first_tile, self.tiles = first_tile, tiles
        self.units_before, self.chunks_before = units_before, chunks_before
        assert self.pieces % OUT_SLOTS == 0 and self.units % 2 == 0
        self.runs = []
        for p in range(self.pieces):
            part, runs = pairs[p * PIECE:(p + 1) * PIECE], []
            for at, (i, j) in enumerate(part):
                if runs and runs[-1][0] == i:
                    runs[-1][2] += 1
                else:
                    runs.append([i, j, 1, at])
            self.runs.append(runs)

    def unit_rows(self, u):
        return self.rows[u * UNIT_ROWS:(u + 1) * UNIT_ROWS]

    def unit_of(self, i):
        return (i - self.rows[0]) // UNIT_ROWS

    def piece_pairs(self, p):
        return min(PIECE, self.pairs - p * PIECE)

    def units_starting(self, p):
        return [self.unit_of(i) for i, j, _, _ in self.runs[p]
                if j == i + 1 and i == self.unit_rows(self.unit_of(i))[0]]

    def slot_uses(self, t, u):
        return self.units_before // 2 + (t - self.first_tile) * (self.units // 2) + u // 2


def pair_products_kernel(nc, x, w, out):
    f32, f32r = mybir.dt.float32, mybir.dt.float32r
    ALU = mybir.AluOpType

    B, F, E = x.shape
    TILES = B // P
    CUT = 7
    ph0 = Phase(0, CUT, F, 0, TILES, 0, 0)
    ph1 = Phase(CUT, F - 1, F, TILES, TILES, TILES * ph0.units, ph0.pieces)
    assert ph0.pieces == ph1.pieces and TILES % 2 == 0 and E == P
    PIECES = ph0.pieces
    W_PAIRS = max(ph0.pairs, ph1.pairs)
    GROUP_USES = PIECES // 2
    SLOT_USES = PIECES // OUT_SLOTS

    x_v = x.rearrange("(t p) f e -> t p (f e)", p=P)
    w_v = w.rearrange("q e f -> e q f")
    out_v = out.rearrange("(t p) q f -> t p (q f)", p=P)

    with ExitStack() as ctx:
        def sb(name, shape, dt):
            return ctx.enter_context(nc.sbuf_tensor(name, shape, dt))

        def ps(name, shape):
            return ctx.enter_context(nc.psum_tensor(name, shape, f32))

        def sem(name):
            return ctx.enter_context(nc.semaphore(name))

        w_hi = sb("w_hi", [P, W_PAIRS * E], f32r)
        w_lo = sb("w_lo", [P, W_PAIRS * E], f32r)
        w_raw = [sb(f"w_raw{i}", [P, PIECE * E], f32) for i in range(2)]
        x_sb = [sb(f"x_sb{i}", [P, F * E], f32) for i in range(2)]
        x_split = [sb(f"x_split{i}", [P, UNIT_ROWS, 2, E], f32) for i in range(2)]
        xT = [sb(f"xT{i}", [P, UNIT_ROWS, 2, P], f32r) for i in range(2)]
        out_sb = [sb(f"out_sb{i}", [P, PIECE * E], f32) for i in range(OUT_SLOTS)]
        ident = sb("ident", [P, P], f32)
        ones = sb("ones", [P, UNIT_ROWS, E], f32)

        prod_ps = [ps(f"prod_ps{i}", [P, PIECE * E]) for i in range(2)]
        xT_ps = [ps(f"xT_ps{i}", [P, UNIT_ROWS, 2, P]) for i in range(2)]

        ident_zero = sem("ident_zero")
        ident_ready = sem("ident_ready")
        ones_ready = sem("ones_ready")
        x_loaded = [sem(f"x_loaded{i}") for i in range(2)]
        w_loaded = [sem(f"w_loaded{i}") for i in range(2)]
        w_hi_ready = sem("w_hi_ready")
        w_ready = sem("w_ready")
        x_hi_ready = sem("x_hi_ready")
        x_split_ready = [sem(f"x_split_ready{i}") for i in range(2)]
        transposed = [sem(f"transposed{i}") for i in range(2)]
        xT_ready = [sem(f"xT_ready{i}") for i in range(2)]
        prod_ready = sem("prod_ready")
        piece_done = [sem(f"piece_done{i}") for i in range(2)]
        out_sent = [sem(f"out_sent{i}") for i in range(OUT_SLOTS)]

        block = ctx.enter_context(nc.Block())

        @block.sync
        def _(sp):
            def load_x(ph, t, buf):
                cols = slice(ph.rows[0] * E, F * E)
                sp.dma_start(x_sb[buf][:, cols], x_v[t - ph.first_tile, :, cols]).then_inc(x_loaded[buf], 16)

            def load_w(ph, c):
                q, n = c * PIECE, ph.piece_pairs(c)
                k = ph.chunks_before + c
                if k >= 2:
                    sp.wait_ge(w_ready, k - 1)
                sp.dma_start(w_raw[k % 2][:, 0:n * E].rearrange("e (q f) -> e q f", f=E),
                             w_v[:, ph.first_pair + q:ph.first_pair + q + n, :]).then_inc(w_loaded[k % 2], 16)

            def send_piece(ph, t, p):
                n = ph.piece_pairs(p) * E
                c0 = (ph.first_pair + p * PIECE) * E
                sp.wait_ge(piece_done[p % 2], t * GROUP_USES + p // 2 + 2)
                sp.dma_start(out_v[t - ph.first_tile, :, c0:c0 + n],
                             out_sb[p % OUT_SLOTS][:, 0:n]).then_inc(out_sent[p % OUT_SLOTS], 16)

            def send_tile(ph, t):
                for p in range(PIECES):
                    send_piece(ph, t, p)

            def send_tile_and_load_w(ph, t, w_ph):
                for p in range(PIECES):
                    if p + 2 < w_ph.pieces:
                        load_w(w_ph, p + 2)
                    send_piece(ph, t, p)

            load_w(ph0, 0)
            load_x(ph0, 0, 0)
            load_w(ph0, 1)
            load_x(ph0, 1, 1)
            send_tile_and_load_w(ph0, 0, ph0)
            with sp.Fori(0, TILES // 2 - 1) as i:
                load_x(ph0, 2 * i + 2, 0)
                send_tile(ph0, 2 * i + 1)
                load_x(ph0, 2 * i + 3, 1)
                send_tile(ph0, 2 * i + 2)
            load_x(ph1, TILES, 0)
            load_w(ph1, 0)
            load_w(ph1, 1)
            send_tile_and_load_w(ph0, TILES - 1, ph1)
            with sp.Fori(TILES // 2, TILES - 1) as i:
                load_x(ph1, 2 * i + 1, 1)
                send_tile(ph1, 2 * i)
                load_x(ph1, 2 * i + 2, 0)
                send_tile(ph1, 2 * i + 1)
            load_x(ph1, 2 * TILES - 1, 1)
            send_tile(ph1, 2 * TILES - 2)
            send_tile(ph1, 2 * TILES - 1)
            for s in range(OUT_SLOTS):
                sp.wait_ge(out_sent[s], 2 * TILES * SLOT_USES * 16)

        @block.gpsimd
        def _(pool):
            nc.gpsimd.memset(ident[:], 0.0).then_inc(ident_zero, 1)
            nc.gpsimd.memset(ones[:], 1.0).then_inc(ones_ready, 1)
            pool.wait_ge(ident_zero, 1)
            nc.gpsimd.affine_select(out=ident[:], in_=ident[:], compare_op=ALU.not_equal, fill=1.0, base=0,
                                    pattern=[[-1, P]], channel_multiplier=1).then_inc(ident_ready, 1)

            pool.wait_ge(ones_ready, 1)

            def split_x(ph, t, buf, loads):
                pool.wait_ge(x_loaded[buf], loads * 16)
                for u in range(ph.units):
                    s, rows = u % 2, ph.unit_rows(u)
                    n = len(rows)
                    raw = x_sb[buf][:, rows[0] * E:(rows[0] + n) * E].rearrange("p (r e) -> p r e", e=E)
                    hi, lo = (x_split[s][:, 0:n, h, :].bitcast(f32r) for h in range(2))
                    pool.wait_ge(transposed[s], ph.slot_uses(t, u) + 1)
                    nc.gpsimd.tensor_tensor(hi, raw, ones[:, 0:n, :], ALU.mult).then_inc(x_hi_ready, 1)
                    pool.wait_ge(x_hi_ready, ph.units_before + (t - ph.first_tile) * ph.units + u + 1)
                    nc.gpsimd.tensor_tensor(lo, raw, x_split[s][:, 0:n, 0, :], ALU.subtract).then_inc(x_split_ready[s], 1)

            for ph in (ph0, ph1):
                with pool.Fori(ph.first_tile // 2, (ph.first_tile + TILES) // 2) as i:
                    split_x(ph, 2 * i, 0, i + 1)
                    split_x(ph, 2 * i + 1, 1, i + 1)

        @block.tensor
        def _(pe):
            def transpose_unit(ph, t, u):
                s = u % 2
                pe.wait_ge(x_split_ready[s], ph.slot_uses(t, u) + 1)
                for r in range(len(ph.unit_rows(u))):
                    for h in range(2):
                        last = nc.tensor.transpose(xT_ps[s][:, r, h, :], x_split[s][:, r, h, :], ident[:])
                last.then_inc(transposed[s], 1)

            def piece_products(ph, t, p, next_unit):
                prods = prod_ps[p % 2]
                pe.wait_ge(w_ready, ph.chunks_before + p + 1)
                pe.wait_ge(piece_done[p % 2], t * GROUP_USES + p // 2 + 1)
                starting = ph.units_starting(p)
                for i, j, n, at in ph.runs[p]:
                    u = ph.unit_of(i)
                    s, r = u % 2, (i - ph.rows[0]) % UNIT_ROWS
                    if u in starting and j == i + 1 and r == 0:
                        next_unit(u)
                        pe.wait_ge(xT_ready[s], ph.slot_uses(t, u) + 1)
                    cuts = [at] + [k for k in range(0, PIECE, BANK_PAIRS) if at < k < at + n] + [at + n]
                    parts = list(zip(cuts, cuts[1:]))
                    for h, w_parts in ((0, (w_hi, w_lo)), (1, (w_hi,))):
                        for a, b in parts:
                            for wt in w_parts:
                                last = nc.tensor.matmul(
                                    prods[:, a * E:b * E], xT[s][:, r, h, :],
                                    wt[:, (p * PIECE + a) * E:(p * PIECE + b) * E],
                                    start=(h == 0 and wt is w_hi), stop=(h == 1),
                                    skip_group_check=True)
                last.then_inc(prod_ready, 1)

            def tile_products(ph, t, following):
                def next_unit(u):
                    if u + 1 < ph.units:
                        transpose_unit(ph, t, u + 1)
                    elif following:
                        transpose_unit(following, t + 1, 0)
                for p in range(PIECES):
                    piece_products(ph, t, p, next_unit)

            for slot in transposed:
                pe.sem_inc(slot, 1)
            pe.wait_ge(ident_ready, 1)
            transpose_unit(ph0, 0, 0)
            with pe.Fori(0, TILES - 1) as t:
                tile_products(ph0, t, ph0)
            tile_products(ph0, TILES - 1, ph1)
            with pe.Fori(TILES, 2 * TILES - 1) as t:
                tile_products(ph1, t, ph1)
            tile_products(ph1, 2 * TILES - 1, None)

        @block.scalar
        def _(act):
            def copy_transposed(ph, t, u):
                s, n = u % 2, len(ph.unit_rows(u))
                act.wait_ge(transposed[s], ph.slot_uses(t, u) + 2)
                nc.scalar.copy(xT[s][:, 0:n, :, :], xT_ps[s][:, 0:n, :, :]).then_inc(xT_ready[s], 1)

            def round_w(ph, c):
                k, n = ph.chunks_before + c, ph.piece_pairs(c) * E
                act.wait_ge(w_loaded[k % 2], (k // 2 + 1) * 16)
                nc.scalar.copy(w_hi[:, c * PIECE * E:c * PIECE * E + n], w_raw[k % 2][:, 0:n]).then_inc(w_hi_ready, 1)

            round_w(ph0, 0)
            copy_transposed(ph0, 0, 0)
            for p in range(PIECES):
                if p + 1 < PIECES:
                    round_w(ph0, p + 1)
                for u in ph0.units_starting(p):
                    if u + 1 < ph0.units:
                        copy_transposed(ph0, 0, u + 1)
            with act.Fori(1, TILES - 1) as t:
                for u in range(ph0.units):
                    copy_transposed(ph0, t, u)
            copy_transposed(ph0, TILES - 1, 0)
            for p in range(PIECES):
                for u in ph0.units_starting(p):
                    if u + 1 < ph0.units:
                        copy_transposed(ph0, TILES - 1, u + 1)
                act.wait_ge(prod_ready, (TILES - 1) * PIECES + p + 1)
                round_w(ph1, p)
            with act.Fori(TILES, 2 * TILES) as t:
                for u in range(ph1.units):
                    copy_transposed(ph1, t, u)

        @block.vector
        def _(dve):
            def split_w(ph, c):
                k, n = ph.chunks_before + c, ph.piece_pairs(c) * E
                cols = slice(c * PIECE * E, c * PIECE * E + n)
                dve.wait_ge(w_hi_ready, k + 1)
                nc.vector.tensor_tensor(w_lo[:, cols], w_raw[k % 2][:, 0:n], w_hi[:, cols].bitcast(f32),
                                        ALU.subtract).then_inc(w_ready, 1)

            def scale_piece(ph, t, buf, p):
                slot = p % OUT_SLOTS
                dve.wait_ge(prod_ready, t * PIECES + p + 1)
                if isinstance(t, int) and t * SLOT_USES + p // OUT_SLOTS == 0:
                    pass
                else:
                    dve.wait_ge(out_sent[slot], (t * SLOT_USES + p // OUT_SLOTS) * 16)
                for i, j, n, at in ph.runs[p]:
                    last = nc.vector.tensor_tensor(out_sb[slot][:, at * E:(at + n) * E],
                                                   prod_ps[p % 2][:, at * E:(at + n) * E],
                                                   x_sb[buf][:, j * E:(j + n) * E], ALU.mult)
                last.then_inc(piece_done[p % 2], 1)

            def scale_tile(ph, t, buf, loads):
                dve.wait_ge(x_loaded[buf], loads * 16)
                for p in range(PIECES):
                    scale_piece(ph, t, buf, p)

            for group in piece_done:
                dve.sem_inc(group, 1)
            split_w(ph0, 0)
            dve.wait_ge(x_loaded[0], 16)
            for p in range(PIECES):
                if p + 1 < PIECES:
                    split_w(ph0, p + 1)
                scale_piece(ph0, 0, 0, p)
            with dve.Fori(0, TILES // 2 - 1) as i:
                scale_tile(ph0, 2 * i + 1, 1, i + 1)
                scale_tile(ph0, 2 * i + 2, 0, i + 2)
            dve.wait_ge(x_loaded[1], TILES // 2 * 16)
            for p in range(PIECES):
                scale_piece(ph0, TILES - 1, 1, p)
                split_w(ph1, p)
            with dve.Fori(TILES // 2, TILES) as i:
                scale_tile(ph1, 2 * i, 0, i + 1)
                scale_tile(ph1, 2 * i + 1, 1, i + 1)


def kernel(r_x, L0_rec_W):
    import numpy as np
    import concourse.bacc as bacc
    from concourse.bass_utils import run_bass_kernel_spmd

    nc = bacc.Bacc("TRN2", target_bir_lowering=False, num_devices=1, dynamic_dma_scratch_size=1024)
    x, w = np.ascontiguousarray(r_x), np.ascontiguousarray(L0_rec_W)
    f32 = mybir.dt.float32
    x_d = nc.dram_tensor("x_dram", x.shape, f32, kind="ExternalInput").ap()
    w_d = nc.dram_tensor("w_dram", w.shape, f32, kind="ExternalInput").ap()
    out_d = nc.dram_tensor("out_dram", (x.shape[0], w.shape[0], w.shape[2]), f32, kind="ExternalOutput").ap()
    pair_products_kernel(nc, x_d, w_d, out_d)
    r = run_bass_kernel_spmd(nc, [{"x_dram": x, "w_dram": w}], core_ids=[0])
    return r.results[0]["out_dram"]
```

```python
import concourse.bass as bass
from concourse import mybir
from contextlib import ExitStack

P = 128
BANK_PAIRS = 4
PIECE_BANKS = 3
PIECE = BANK_PAIRS * PIECE_BANKS
UNIT_ROWS = 2
OUT_SLOTS = 4
W_SLOTS = 3
SPLIT_SLOTS = 4


class Phase:

    def __init__(self, first, last, fields, first_tile, tiles, units_before, chunks_before):
        self.rows = list(range(first, last))
        self.first_pair = sum(fields - 1 - i for i in range(first))
        pairs = [(i, j) for i in self.rows for j in range(i + 1, fields)]
        self.pairs = len(pairs)
        sizes = [PIECE] * (self.pairs // PIECE) + [self.pairs % PIECE]
        if sizes[-1] <= BANK_PAIRS:
            sizes[-2:] = [sizes[-2] - BANK_PAIRS, sizes[-1] + BANK_PAIRS]
        self.pieces = len(sizes)
        self.starts = [sum(sizes[:p]) for p in range(self.pieces + 1)]
        self.units = -(-len(self.rows) // UNIT_ROWS)
        self.first_tile, self.tiles = first_tile, tiles
        self.units_before, self.chunks_before = units_before, chunks_before
        assert self.pieces % OUT_SLOTS == 0 and self.units % SPLIT_SLOTS == 0
        self.runs = []
        for p in range(self.pieces):
            part, runs = pairs[self.starts[p]:self.starts[p + 1]], []
            for at, (i, j) in enumerate(part):
                if runs and runs[-1][0] == i:
                    runs[-1][2] += 1
                else:
                    runs.append([i, j, 1, at])
            self.runs.append(runs)

    def unit_rows(self, u):
        return self.rows[u * UNIT_ROWS:(u + 1) * UNIT_ROWS]

    def unit_of(self, i):
        return (i - self.rows[0]) // UNIT_ROWS

    def piece_pairs(self, p):
        return self.starts[p + 1] - self.starts[p]

    def units_starting(self, p):
        return [self.unit_of(i) for i, j, _, _ in self.runs[p]
                if j == i + 1 and i == self.unit_rows(self.unit_of(i))[0]]

    def batch_tile(self, t):
        return t * -1 + (2 * self.tiles - 1) if self.first_tile else t

    def slot_uses(self, t, u):
        return self.units_before // 2 + (t - self.first_tile) * (self.units // 2) + u // 2


def pair_products_kernel(nc, x, w, out):
    f32, f32r = mybir.dt.float32, mybir.dt.float32r
    ALU = mybir.AluOpType

    B, F, E = x.shape
    TILES = B // P
    CUT = 7
    ph0 = Phase(0, CUT, F, 0, TILES, 0, 0)
    ph1 = Phase(CUT, F - 1, F, TILES, TILES, TILES * ph0.units, ph0.pieces)
    assert ph0.pieces == ph1.pieces and TILES % 2 == 0 and E == P
    PIECES = ph0.pieces
    W_PAIRS = max(ph0.pairs, ph1.pairs)
    GROUP_USES = PIECES // 2
    SLOT_USES = PIECES // OUT_SLOTS

    x_v = x.rearrange("(t p) f e -> t p (f e)", p=P)
    w_v = w.rearrange("q e f -> e q f")
    out_v = out.rearrange("(t p) q f -> t p (q f)", p=P)

    with ExitStack() as ctx:
        def sb(name, shape, dt):
            return ctx.enter_context(nc.sbuf_tensor(name, shape, dt))

        def ps(name, shape):
            return ctx.enter_context(nc.psum_tensor(name, shape, f32))

        def sem(name):
            return ctx.enter_context(nc.semaphore(name))

        w_hi = sb("w_hi", [P, W_PAIRS * E], f32r)
        w_lo = sb("w_lo", [P, W_PAIRS * E], f32r)
        w_raw = [sb(f"w_raw{i}", [P, PIECE * E], f32) for i in range(W_SLOTS)]
        x_sb = [sb(f"x_sb{i}", [P, F * E], f32) for i in range(2)]
        x_split = [sb(f"x_split{i}", [P, UNIT_ROWS, 2, E], f32) for i in range(SPLIT_SLOTS)]
        xT = [sb(f"xT{i}", [P, UNIT_ROWS, 2, P], f32r) for i in range(SPLIT_SLOTS)]
        out_sb = [sb(f"out_sb{i}", [P, PIECE * E], f32) for i in range(OUT_SLOTS)]
        ident = sb("ident", [P, P], f32)
        one = sb("one", [P, 1, 1], f32)

        prod_ps = [ps(f"prod_ps{i}", [P, PIECE * E]) for i in range(2)]
        xT_ps = [ps(f"xT_ps{i}", [P, UNIT_ROWS, 2, P]) for i in range(2)]

        ident_zero = sem("ident_zero")
        ident_ready = sem("ident_ready")
        one_ready = sem("one_ready")
        x_loaded = [sem(f"x_loaded{i}") for i in range(2)]
        x_rest_loaded = sem("x_rest_loaded")
        w_loaded = [sem(f"w_loaded{i}") for i in range(W_SLOTS)]
        w_hi_ready = sem("w_hi_ready")
        w_ready = sem("w_ready")
        x_hi_ready = sem("x_hi_ready")
        x_split_ready = [sem(f"x_split_ready{i}") for i in range(2)]
        transposed = [sem(f"transposed{i}") for i in range(2)]
        xT_ready = [sem(f"xT_ready{i}") for i in range(2)]
        prod_ready = sem("prod_ready")
        piece_done = [sem(f"piece_done{i}") for i in range(2)]
        out_sent = [sem(f"out_sent{i}") for i in range(OUT_SLOTS)]

        block = ctx.enter_context(nc.Block())

        @block.sync
        def _(sp):
            def load_x(ph, t, buf):
                cols = slice(ph.rows[0] * E, F * E)
                sp.dma_start(x_sb[buf][:, cols], x_v[ph.batch_tile(t), :, cols]).then_inc(x_loaded[buf], 16)

            def load_w(ph, c):
                q, n = ph.starts[c], ph.piece_pairs(c)
                k = ph.chunks_before + c
                if k >= W_SLOTS:
                    sp.wait_ge(w_ready, k - W_SLOTS + 1)
                sp.dma_start(w_raw[k % W_SLOTS][:, 0:n * E].rearrange("e (q f) -> e q f", f=E),
                             w_v[:, ph.first_pair + q:ph.first_pair + q + n, :]).then_inc(w_loaded[k % W_SLOTS], 16)

            def send_piece(ph, t, p):
                n = ph.piece_pairs(p) * E
                c0 = (ph.first_pair + ph.starts[p]) * E
                sp.wait_ge(piece_done[p % 2], t * GROUP_USES + p // 2 + 2)
                sp.dma_start(out_v[ph.batch_tile(t), :, c0:c0 + n],
                             out_sb[p % OUT_SLOTS][:, 0:n]).then_inc(out_sent[p % OUT_SLOTS], 16)

            def send_tile(ph, t):
                for p in range(PIECES):
                    send_piece(ph, t, p)

            def send_tile_and_load_w(ph, t, w_ph, before_piece):
                for p in range(PIECES):
                    if p + W_SLOTS < w_ph.pieces:
                        load_w(w_ph, p + W_SLOTS)
                    if p in before_piece:
                        before_piece[p]()
                    send_piece(ph, t, p)

            load_w(ph0, 0)
            first = (PIECE + 1) * E
            sp.dma_start(x_sb[0][:, 0:first], x_v[0, :, 0:first]).then_inc(x_loaded[0], 16)
            load_w(ph0, 1)
            sp.dma_start(x_sb[0][:, first:], x_v[0, :, first:]).then_inc(x_rest_loaded, 16)
            for c in range(2, W_SLOTS):
                load_w(ph0, c)
            send_tile_and_load_w(ph0, 0, ph0, {2: lambda: load_x(ph0, 1, 1)})
            with sp.Fori(0, TILES // 2 - 1) as i:
                load_x(ph0, 2 * i + 2, 0)
                send_tile(ph0, 2 * i + 1)
                load_x(ph0, 2 * i + 3, 1)
                send_tile(ph0, 2 * i + 2)
            for c in range(W_SLOTS):
                load_w(ph1, c)
            send_tile_and_load_w(ph0, TILES - 1, ph1, {})
            send_tile(ph1, TILES)
            with sp.Fori(TILES // 2, TILES - 1) as i:
                load_x(ph1, 2 * i + 2, 1)
                send_tile(ph1, 2 * i + 1)
                load_x(ph1, 2 * i + 3, 0)
                send_tile(ph1, 2 * i + 2)
            send_tile(ph1, 2 * TILES - 1)
            for s in range(OUT_SLOTS):
                sp.wait_ge(out_sent[s], 2 * TILES * SLOT_USES * 16)

        @block.gpsimd
        def _(pool):
            nc.gpsimd.memset(ident[:], 0.0).then_inc(ident_zero, 1)
            nc.gpsimd.memset(one[:], 1.0).then_inc(one_ready, 1)
            pool.wait_ge(ident_zero, 1)
            nc.gpsimd.affine_select(out=ident[:], in_=ident[:], compare_op=ALU.not_equal, fill=1.0, base=0,
                                    pattern=[[-1, P]], channel_multiplier=1).then_inc(ident_ready, 1)

            pool.wait_ge(one_ready, 1)

            def split_x(ph, t, buf, loads):
                pool.wait_ge(x_loaded[buf], loads * 16)
                for u in range(ph.units):
                    s, rows = u % SPLIT_SLOTS, ph.unit_rows(u)
                    n = len(rows)
                    raw = x_sb[buf][:, rows[0] * E:(rows[0] + n) * E].rearrange("p (r e) -> p r e", e=E)
                    hi, lo = (x_split[s][:, 0:n, h, :].bitcast(f32r) for h in range(2))
                    pool.wait_ge(transposed[u % 2], ph.slot_uses(t, u) + 1)
                    nc.gpsimd.tensor_tensor(hi, raw, one[:].to_broadcast([P, n, E]), ALU.mult).then_inc(x_hi_ready, 1)
                    pool.wait_ge(x_hi_ready, ph.units_before + (t - ph.first_tile) * ph.units + u + 1)
                    nc.gpsimd.tensor_tensor(lo, raw, x_split[s][:, 0:n, 0, :], ALU.subtract).then_inc(x_split_ready[u % 2], 1)

            with pool.Fori(0, TILES // 2) as i:
                split_x(ph0, 2 * i, 0, i + 1)
                split_x(ph0, 2 * i + 1, 1, i + 1)
            with pool.Fori(TILES // 2, TILES) as i:
                split_x(ph1, 2 * i, 1, i)
                split_x(ph1, 2 * i + 1, 0, i)

        @block.tensor
        def _(pe):
            def transpose_unit(ph, t, u):
                s = u % 2
                pe.wait_ge(x_split_ready[s], ph.slot_uses(t, u) + 1)
                for r in range(len(ph.unit_rows(u))):
                    for h in range(2):
                        last = nc.tensor.transpose(xT_ps[s][:, r, h, :], x_split[u % SPLIT_SLOTS][:, r, h, :], ident[:])
                last.then_inc(transposed[s], 1)

            def piece_products(ph, t, p, transpose_ahead):
                prods = prod_ps[p % 2]
                pe.wait_ge(w_ready, ph.chunks_before + p + 1)
                pe.wait_ge(piece_done[p % 2], t * GROUP_USES + p // 2 + 1)
                starting = ph.units_starting(p)
                for i, j, n, at in ph.runs[p]:
                    u = ph.unit_of(i)
                    r = (i - ph.rows[0]) % UNIT_ROWS
                    if u in starting and j == i + 1 and r == 0:
                        pe.wait_ge(xT_ready[u % 2], ph.slot_uses(t, u) + 1)
                        transpose_ahead(u)
                    cuts = [at] + [k for k in range(0, PIECE, BANK_PAIRS) if at < k < at + n] + [at + n]
                    parts = list(zip(cuts, cuts[1:]))
                    for h, w_parts in ((0, (w_hi, w_lo)), (1, (w_hi,))):
                        for a, b in parts:
                            for wt in w_parts:
                                last = nc.tensor.matmul(
                                    prods[:, a * E:b * E], xT[u % SPLIT_SLOTS][:, r, h, :],
                                    wt[:, (ph.starts[p] + a) * E:(ph.starts[p] + b) * E],
                                    start=(h == 0 and wt is w_hi), stop=(h == 1),
                                    skip_group_check=True)
                last.then_inc(prod_ready, 1)

            def tile_products(ph, t, following):
                def transpose_ahead(u):
                    if u + 2 < ph.units:
                        transpose_unit(ph, t, u + 2)
                    elif following:
                        transpose_unit(following, t + 1, u + 2 - ph.units)
                for p in range(PIECES):
                    piece_products(ph, t, p, transpose_ahead)

            for slot in transposed:
                pe.sem_inc(slot, SPLIT_SLOTS // 2)
            pe.wait_ge(ident_ready, 1)
            for u in range(2):
                transpose_unit(ph0, 0, u)
            with pe.Fori(0, TILES - 1) as t:
                tile_products(ph0, t, ph0)
            tile_products(ph0, TILES - 1, ph1)
            with pe.Fori(TILES, 2 * TILES - 1) as t:
                tile_products(ph1, t, ph1)
            tile_products(ph1, 2 * TILES - 1, None)

        @block.scalar
        def _(act):
            def copy_transposed(ph, t, u):
                s, n = u % 2, len(ph.unit_rows(u))
                act.wait_ge(transposed[s], SPLIT_SLOTS // 2 + ph.slot_uses(t, u) + 1)
                nc.scalar.copy(xT[u % SPLIT_SLOTS][:, 0:n, :, :], xT_ps[s][:, 0:n, :, :]).then_inc(xT_ready[s], 1)

            def round_w(ph, c):
                k, n = ph.chunks_before + c, ph.piece_pairs(c) * E
                act.wait_ge(w_loaded[k % W_SLOTS], (k // W_SLOTS + 1) * 16)
                nc.scalar.copy(w_hi[:, ph.starts[c] * E:ph.starts[c] * E + n], w_raw[k % W_SLOTS][:, 0:n]).then_inc(w_hi_ready, 1)

            round_w(ph0, 0)
            for u in range(2):
                copy_transposed(ph0, 0, u)
            for p in range(PIECES):
                if p + 1 < PIECES:
                    round_w(ph0, p + 1)
                for u in ph0.units_starting(p):
                    if u + 2 < ph0.units:
                        copy_transposed(ph0, 0, u + 2)
            with act.Fori(1, TILES - 1) as t:
                for u in range(ph0.units):
                    copy_transposed(ph0, t, u)
            for u in range(2):
                copy_transposed(ph0, TILES - 1, u)
            for p in range(PIECES):
                for u in ph0.units_starting(p):
                    if u + 2 < ph0.units:
                        copy_transposed(ph0, TILES - 1, u + 2)
                act.wait_ge(prod_ready, (TILES - 1) * PIECES + p + 1)
                round_w(ph1, p)
            with act.Fori(TILES, 2 * TILES) as t:
                for u in range(ph1.units):
                    copy_transposed(ph1, t, u)

        @block.vector
        def _(dve):
            def split_w(ph, c):
                k, n = ph.chunks_before + c, ph.piece_pairs(c) * E
                cols = slice(ph.starts[c] * E, ph.starts[c] * E + n)
                dve.wait_ge(w_hi_ready, k + 1)
                nc.vector.tensor_tensor(w_lo[:, cols], w_raw[k % W_SLOTS][:, 0:n], w_hi[:, cols].bitcast(f32),
                                        ALU.subtract).then_inc(w_ready, 1)

            def scale_piece(ph, t, buf, p):
                slot = p % OUT_SLOTS
                dve.wait_ge(prod_ready, t * PIECES + p + 1)
                if isinstance(t, int) and t * SLOT_USES + p // OUT_SLOTS == 0:
                    pass
                else:
                    dve.wait_ge(out_sent[slot], (t * SLOT_USES + p // OUT_SLOTS) * 16)
                for i, j, n, at in ph.runs[p]:
                    last = nc.vector.tensor_tensor(out_sb[slot][:, at * E:(at + n) * E],
                                                   prod_ps[p % 2][:, at * E:(at + n) * E],
                                                   x_sb[buf][:, j * E:(j + n) * E], ALU.mult)
                last.then_inc(piece_done[p % 2], 1)

            def scale_tile(ph, t, buf, loads):
                dve.wait_ge(x_loaded[buf], loads * 16)
                for p in range(PIECES):
                    scale_piece(ph, t, buf, p)

            for group in piece_done:
                dve.sem_inc(group, 1)
            split_w(ph0, 0)
            dve.wait_ge(x_loaded[0], 16)
            for p in range(PIECES):
                if p + 1 < PIECES:
                    split_w(ph0, p + 1)
                if p == 1:
                    dve.wait_ge(x_rest_loaded, 16)
                scale_piece(ph0, 0, 0, p)
            with dve.Fori(0, TILES // 2 - 1) as i:
                scale_tile(ph0, 2 * i + 1, 1, i + 1)
                scale_tile(ph0, 2 * i + 2, 0, i + 2)
            dve.wait_ge(x_loaded[1], TILES // 2 * 16)
            for p in range(PIECES):
                scale_piece(ph0, TILES - 1, 1, p)
                split_w(ph1, p)
            with dve.Fori(TILES // 2, TILES) as i:
                scale_tile(ph1, 2 * i, 1, i)
                scale_tile(ph1, 2 * i + 1, 0, i)


def kernel(r_x, L0_rec_W):
    import numpy as np
    import concourse.bacc as bacc
    from concourse.bass_utils import run_bass_kernel_spmd

    nc = bacc.Bacc("TRN2", target_bir_lowering=False, num_devices=1, dynamic_dma_scratch_size=1024)
    x, w = np.ascontiguousarray(r_x), np.ascontiguousarray(L0_rec_W)
    f32 = mybir.dt.float32
    x_d = nc.dram_tensor("x_dram", x.shape, f32, kind="ExternalInput").ap()
    w_d = nc.dram_tensor("w_dram", w.shape, f32, kind="ExternalInput").ap()
    out_d = nc.dram_tensor("out_dram", (x.shape[0], w.shape[0], w.shape[2]), f32, kind="ExternalOutput").ap()
    pair_products_kernel(nc, x_d, w_d, out_d)
    r = run_bass_kernel_spmd(nc, [{"x_dram": x, "w_dram": w}], core_ids=[0])
    return r.results[0]["out_dram"]
```

```python
import concourse.bass as bass
from concourse import mybir
from contextlib import ExitStack

P = 128
PAIR = 2
BANK_PAIRS = 4
CHUNK = 8
UNIT_ROWS = 2
SPLIT_SLOTS = 3
GROUPS = 3
OUT_SLOTS = 6
W_AHEAD = 8
X_GROUPS = [(0, 4), (4, 8), (8, 12), (12, 16), (16, 19), (19, 24)]


class Plan:

    def __init__(self, fields):
        pairs = [(i, j) for i in range(fields) for j in range(i + 1, fields)]
        self.pairs = len(pairs)
        short = 1
        while (self.pairs - short * BANK_PAIRS) % CHUNK or \
                ((self.pairs - short * BANK_PAIRS) // CHUNK + short) % SPLIT_SLOTS:
            short += 1
        sizes = [BANK_PAIRS] + [CHUNK] * ((self.pairs - short * BANK_PAIRS) // CHUNK) + [BANK_PAIRS] * (short - 1)
        self.chunks = len(sizes)
        self.starts = [sum(sizes[:c]) for c in range(self.chunks + 1)]
        assert self.starts[-1] == self.pairs
        self.pieces = PAIR * self.chunks
        assert self.pieces % GROUPS == 0 and self.pieces % OUT_SLOTS == 0
        self.units = -(-(fields - 1) // UNIT_ROWS)
        self.rows = fields - 1
        self.runs = []
        for c in range(self.chunks):
            runs = []
            for at, (i, j) in enumerate(pairs[self.starts[c]:self.starts[c + 1]]):
                if runs and runs[-1][0] == i:
                    runs[-1][2] += 1
                else:
                    runs.append([i, j, 1, at])
            self.runs.append(runs)
        self.last_chunk = [max(c for c in range(self.chunks) if any(r[0] == i for r in self.runs[c]))
                           for i in range(self.rows)]

    def size(self, c):
        return self.starts[c + 1] - self.starts[c]

    def unit_rows(self, u):
        return range(u * UNIT_ROWS, min((u + 1) * UNIT_ROWS, self.rows))

    def unit_starting(self, run):
        i, j, _, _ = run
        return i // UNIT_ROWS if j == i + 1 and i % UNIT_ROWS == 0 else None

    def units_starting(self, c):
        return [u for run in self.runs[c] if (u := self.unit_starting(run)) is not None]


def x_group(field):
    return next(g for g, (a, b) in enumerate(X_GROUPS) if a <= field < b)


def pair_products_kernel(nc, x, w, out):
    f32, f32r = mybir.dt.float32, mybir.dt.float32r
    ALU = mybir.AluOpType

    B, F, E = x.shape
    PASSES = B // (P * PAIR)
    plan = Plan(F)
    CHUNKS, PIECES, UNITS = plan.chunks, plan.pieces, plan.units
    GROUP_USES, SLOT_USES = PIECES // GROUPS, PIECES // OUT_SLOTS
    assert E == P and X_GROUPS[-1][1] == F

    x_v = x.rearrange("(s t p) f e -> s p t (f e)", t=PAIR, p=P)
    w_v = w.rearrange("q e f -> e q f")
    out_v = out.rearrange("(s t p) q f -> s t p (q f)", t=PAIR, p=P)

    with ExitStack() as ctx:
        def sb(name, shape, dt):
            return ctx.enter_context(nc.sbuf_tensor(name, shape, dt))

        def ps(name, shape):
            return ctx.enter_context(nc.psum_tensor(name, shape, f32))

        def sem(name):
            return ctx.enter_context(nc.semaphore(name))

        w_sb = sb("w_sb", [P, plan.pairs * E], f32)
        w_hi = [sb(f"w_hi{k}", [P, CHUNK * E], f32r) for k in range(SPLIT_SLOTS)]
        w_lo = [sb(f"w_lo{k}", [P, CHUNK * E], f32r) for k in range(SPLIT_SLOTS)]
        x_sb = sb("x_sb", [P, PAIR, F * E], f32)
        xT = [[sb(f"xT{par}{a}", [P, 2, UNIT_ROWS, P], f32r) for a in range(PAIR)] for par in range(2)]
        out_sb = [sb(f"out_sb{k}", [P, CHUNK * E], f32) for k in range(OUT_SLOTS)]
        ident = sb("ident", [P, P], f32)

        prod_ps = [ps(f"prod_ps{k}", [P, CHUNK * E]) for k in range(GROUPS)]
        xT_ps = [ps(f"xT_ps{a}", [P, BANK_PAIRS, P]) for a in range(PAIR)]

        ident_zero = sem("ident_zero")
        ident_ready = sem("ident_ready")
        x_loaded = [sem(f"x_loaded{g}") for g in range(len(X_GROUPS))]
        w_loaded = [sem(f"w_loaded{k}") for k in range(W_AHEAD)]
        w_hi_ready = sem("w_hi_ready")
        w_split = sem("w_split")
        transposed = [sem(f"transposed{a}") for a in range(PAIR)]
        xT_hi_ready = [sem(f"xT_hi_ready{a}") for a in range(PAIR)]
        xT_ready = [sem(f"xT_ready{a}") for a in range(PAIR)]
        prod_ready = sem("prod_ready")
        piece_done = [sem(f"piece_done{k}") for k in range(GROUPS)]
        out_sent = [sem(f"out_sent{k}") for k in range(OUT_SLOTS)]

        block = ctx.enter_context(nc.Block())

        @block.sync
        def _(sp):
            def load_x(s, g):
                a, b = X_GROUPS[g]
                sp.dma_start(x_sb[:, :, a * E:b * E], x_v[s, :, :, a * E:b * E]).then_inc(x_loaded[g], 16)

            def load_w(c):
                a, b = plan.starts[c], plan.starts[c + 1]
                sp.dma_start(w_sb[:, a * E:b * E].rearrange("e (q f) -> e q f", f=E),
                             w_v[:, a:b, :]).then_inc(w_loaded[c % W_AHEAD], 16)

            def send_pass(s, load_all_w=False, load_next_x=True):
                for c in range(CHUNKS):
                    cols = slice(plan.starts[c] * E, plan.starts[c + 1] * E)
                    for a in range(PAIR):
                        q = PAIR * c + a
                        sp.wait_ge(piece_done[q % GROUPS], s * GROUP_USES + q // GROUPS + 2)
                        sp.dma_start(out_v[s, a, :, cols],
                                     out_sb[q % OUT_SLOTS][:, 0:plan.size(c) * E]).then_inc(out_sent[q % OUT_SLOTS], 16)
                    if load_all_w and c + W_AHEAD < CHUNKS:
                        load_w(c + W_AHEAD)
                    if load_next_x:
                        for g, (_, end) in enumerate(X_GROUPS):
                            if plan.last_chunk[min(end, plan.rows) - 1] == c:
                                load_x(s + 1, g)

            load_x(0, 0)
            load_w(0)
            load_x(0, 1)
            load_w(1)
            for g in range(2, len(X_GROUPS)):
                load_x(0, g)
                load_w(g)
            for c in range(len(X_GROUPS), W_AHEAD):
                load_w(c)
            send_pass(0, load_all_w=True)
            with sp.Fori(1, PASSES - 1) as s:
                send_pass(s)
            send_pass(PASSES - 1, load_next_x=False)
            for k in range(OUT_SLOTS):
                sp.wait_ge(out_sent[k], PASSES * SLOT_USES * 16)

        @block.gpsimd
        def _(pool):
            nc.gpsimd.memset(ident[:], 0.0).then_inc(ident_zero, 1)
            pool.wait_ge(ident_zero, 1)
            nc.gpsimd.affine_select(out=ident[:], in_=ident[:], compare_op=ALU.not_equal, fill=1.0, base=0,
                                    pattern=[[-1, P]], channel_multiplier=1).then_inc(ident_ready, 1)
            with pool.Fori(0, PASSES) as s:
                for c in range(CHUNKS):
                    k, n = c % SPLIT_SLOTS, plan.size(c) * E
                    a = plan.starts[c] * E
                    pool.wait_ge(w_hi_ready, s * CHUNKS + c + 1)
                    nc.gpsimd.tensor_tensor(w_lo[k][:, 0:n], w_sb[:, a:a + n], w_hi[k][:, 0:n].bitcast(f32),
                                            ALU.subtract).then_inc(w_split, 1)

        @block.tensor
        def _(pe):
            def transpose_unit(s, u, a):
                rows = plan.unit_rows(u)
                if u == 0 or x_group(rows[-1]) != x_group(rows[0] - 1):
                    pe.wait_ge(x_loaded[x_group(rows[-1])], (s + 1) * 16)
                for r, i in enumerate(rows):
                    last = nc.tensor.transpose(xT_ps[a][:, r, :], x_sb[:, a, i * E:(i + 1) * E], ident[:])
                last.then_inc(transposed[a], 1)

            def piece_products(s, c, a):
                q = PAIR * c + a
                prods, k = prod_ps[q % GROUPS], c % SPLIT_SLOTS
                if a == 0:
                    pe.wait_ge(w_split, s * CHUNKS + c + 1)
                pe.wait_ge(piece_done[q % GROUPS], s * GROUP_USES + q // GROUPS + 1)
                for run in plan.runs[c]:
                    i, _, n, at = run
                    u = plan.unit_starting(run)
                    if u is not None:
                        pe.wait_ge(xT_ready[a], s * UNITS + u + 1)
                        if u + 1 < UNITS:
                            transpose_unit(s, u + 1, a)
                    xt = xT[i // UNIT_ROWS % 2][a]
                    cuts = [at] + [m for m in range(0, CHUNK, BANK_PAIRS) if at < m < at + n] + [at + n]
                    for h, w_parts in ((0, (w_hi[k], w_lo[k])), (1, (w_hi[k],))):
                        for lo, hi in zip(cuts, cuts[1:]):
                            for wt in w_parts:
                                last = nc.tensor.matmul(
                                    prods[:, lo * E:hi * E], xt[:, h, i % UNIT_ROWS, :], wt[:, lo * E:hi * E],
                                    start=(h == 0 and wt is w_hi[k]), stop=(h == 1), skip_group_check=True)
                last.then_inc(prod_ready, 1)

            pe.wait_ge(ident_ready, 1)
            with pe.Fori(0, PASSES) as s:
                for a in range(PAIR):
                    transpose_unit(s, 0, a)
                for c in range(CHUNKS):
                    for a in range(PAIR):
                        piece_products(s, c, a)

        @block.scalar
        def _(act):
            def round_w(s, c, wait_load=False):
                k, n = c % SPLIT_SLOTS, plan.size(c) * E
                a = plan.starts[c] * E
                if wait_load:
                    act.wait_ge(w_loaded[c % W_AHEAD], (c // W_AHEAD + 1) * 16)
                nc.scalar.copy(w_hi[k][:, 0:n], w_sb[:, a:a + n]).then_inc(w_hi_ready, 1)

            def round_xT(s, u, a):
                n = len(plan.unit_rows(u))
                act.wait_ge(transposed[a], s * UNITS + u + 1)
                nc.scalar.copy(xT[u % 2][a][:, 0, 0:n, :], xT_ps[a][:, 0:n, :]).then_inc(xT_hi_ready[a], 1)

            def round_pass(s, first=False, last=False):
                for a in range(PAIR):
                    round_xT(s, 0, a)
                for c in range(CHUNKS):
                    for a in range(PAIR):
                        for u in plan.units_starting(c):
                            if u + 1 < UNITS:
                                round_xT(s, u + 1, a)
                    ahead = c + SPLIT_SLOTS
                    if ahead < CHUNKS or not last:
                        act.wait_ge(prod_ready, s * PIECES + PAIR * (c + 1))
                        round_w(s, ahead % CHUNKS, wait_load=first and ahead < CHUNKS)

            for c in range(SPLIT_SLOTS):
                round_w(0, c, wait_load=True)
            round_pass(0, first=True)
            with act.Fori(1, PASSES - 1) as s:
                round_pass(s)
            round_pass(PASSES - 1, last=True)

        @block.vector
        def _(dve):
            def split_xT(s, u, a):
                n, xt = len(plan.unit_rows(u)), xT[u % 2][a]
                dve.wait_ge(xT_hi_ready[a], s * UNITS + u + 1)
                nc.vector.tensor_tensor(xt[:, 1, 0:n, :], xT_ps[a][:, 0:n, :], xt[:, 0, 0:n, :].bitcast(f32),
                                        ALU.subtract).then_inc(xT_ready[a], 1)

            def scale_pass(s, first=False):
                loaded = set()
                for a in range(PAIR):
                    split_xT(s, 0, a)
                for c in range(CHUNKS):
                    for a in range(PAIR):
                        for u in plan.units_starting(c):
                            if u + 1 < UNITS:
                                split_xT(s, u + 1, a)
                        q = PAIR * c + a
                        for _, j, n, _ in plan.runs[c]:
                            for g in range(x_group(j), x_group(j + n - 1) + 1):
                                if g not in loaded:
                                    dve.wait_ge(x_loaded[g], (s + 1) * 16)
                                    loaded.add(g)
                        if not (first and q < OUT_SLOTS):
                            dve.wait_ge(out_sent[q % OUT_SLOTS], (s * SLOT_USES + q // OUT_SLOTS) * 16)
                        dve.wait_ge(prod_ready, s * PIECES + q + 1)
                        for _, j, n, at in plan.runs[c]:
                            last = nc.vector.tensor_tensor(out_sb[q % OUT_SLOTS][:, at * E:(at + n) * E],
                                                           prod_ps[q % GROUPS][:, at * E:(at + n) * E],
                                                           x_sb[:, a, j * E:(j + n) * E], ALU.mult)
                        last.then_inc(piece_done[q % GROUPS], 1)

            for group in piece_done:
                dve.sem_inc(group, 1)
            scale_pass(0, first=True)
            with dve.Fori(1, PASSES) as s:
                scale_pass(s)


def kernel(r_x, L0_rec_W):
    import numpy as np
    import concourse.bacc as bacc
    from concourse.bass_utils import run_bass_kernel_spmd

    nc = bacc.Bacc("TRN2", target_bir_lowering=False, num_devices=1, dynamic_dma_scratch_size=1024)
    x, w = np.ascontiguousarray(r_x), np.ascontiguousarray(L0_rec_W)
    f32 = mybir.dt.float32
    x_d = nc.dram_tensor("x_dram", x.shape, f32, kind="ExternalInput").ap()
    w_d = nc.dram_tensor("w_dram", w.shape, f32, kind="ExternalInput").ap()
    out_d = nc.dram_tensor("out_dram", (x.shape[0], w.shape[0], w.shape[2]), f32, kind="ExternalOutput").ap()
    pair_products_kernel(nc, x_d, w_d, out_d)
    r = run_bass_kernel_spmd(nc, [{"x_dram": x, "w_dram": w}], core_ids=[0])
    return r.results[0]["out_dram"]
```
